# Optimizing a Trainium2 kernel written in Bass

```python
import numpy as np
import jax
import jax.numpy as jnp

def _softmax(x, axis=-1):
    return jax.nn.softmax(x, axis=axis)

def _gelu(x):
    return jax.nn.gelu(x, approximate=True)

def _silu(x):
    return jax.nn.silu(x)

def _sigmoid(x):
    return jax.nn.sigmoid(x)

def _layernorm(x, axis=-1, eps=1e-05):
    m = jnp.mean(x, axis=axis, keepdims=True)
    v = jnp.var(x, axis=axis, keepdims=True)
    return (x - m) / jnp.sqrt(v + eps)

def _scatter_add(tgt, idx, src, axis=0):
    return tgt.at[idx].add(src)

def _segment_sum(src, seg, n):
    return jax.ops.segment_sum(src, seg, n)
kernel_name = 'mk_rec_standalone_d1_rec_r8_fa3ed5'

def setup_inputs(seed: int=0):
    np.random.seed(seed)
    _w = jnp.asarray

    def _rec_inputs():
        import jax
        import jax.numpy as jnp
        _rk = jax.random.key(seed)
        r_user_embeddings = -0.000928989 + 1.00043 * jax.random.normal(jax.random.fold_in(_rk, 1), (512, 64), jnp.float32)
        r_price_features = 0.00513981 + 1.0024 * jax.random.normal(jax.random.fold_in(_rk, 2), (512, 2), jnp.float32)
        r_temporal_features = -0.0043416 + 0.998921 * jax.random.normal(jax.random.fold_in(_rk, 3), (512, 2), jnp.float32)
        r_item_ids = jax.random.randint(jax.random.fold_in(_rk, 4), (512,), 26, 999969, jnp.int32)
        r_category_ids = jax.random.randint(jax.random.fold_in(_rk, 5), (512,), 0, 1001, jnp.int32)
        r_wf1 = jax.random.randint(jax.random.fold_in(_rk, 6), (512,), 0, 1250, jnp.int32)
        r_wf2 = jax.random.randint(jax.random.fold_in(_rk, 7), (512,), 0, 9999, jnp.int32)
        return (r_user_embeddings, r_price_features, r_temporal_features, r_item_ids, r_category_ids, r_wf1, r_wf2)
    r_user_embeddings, r_price_features, r_temporal_features, r_item_ids, r_category_ids, r_wf1, r_wf2 = _rec_inputs()

    def _L0_rec_setup():
        import jax, jax.numpy as jnp
        import numpy as np
        B = 2048
        NUM_ITEMS = 125000
        NUM_CATS = 1001
        USER_DIM = 64
        ITEM_DIM = 64
        CAT_DIM = 32
        DIM1 = 1250
        DIM2 = 1250
        DEEP_IN = USER_DIM + ITEM_DIM + CAT_DIM + 2 + 2
        HID = [128, 64, 32]
        BN_EPS = 1e-05

        def _bn(x, g, b):
            return x * (g / jnp.sqrt(1.0 + BN_EPS)) + b
        key = jax.random.key(seed)
        ks = jax.random.split(key, 24)
        inp = {'user_embeddings': jax.random.normal(ks[0], (B, USER_DIM), jnp.float32), 'price_features': jax.random.normal(ks[1], (B, 2), jnp.float32), 'temporal_features': jax.random.normal(ks[2], (B, 2), jnp.float32), 'item_emb': jax.random.normal(ks[3], (NUM_ITEMS, ITEM_DIM), jnp.float32) * 0.02, 'cat_emb': jax.random.normal(ks[4], (NUM_CATS, CAT_DIM), jnp.float32) * 0.02, 'wide_emb1': jax.random.normal(ks[5], (DIM1, 1), jnp.float32) * 0.02, 'wide_emb2': jax.random.normal(ks[6], (DIM2, 1), jnp.float32) * 0.02, 'cross_W': jax.random.normal(ks[7], (DIM1 * DIM2,), jnp.float32) * 0.001, 'item_ids': jax.random.randint(ks[8], (B,), 0, NUM_ITEMS), 'category_ids': jax.random.randint(ks[9], (B,), 0, NUM_CATS), 'wf1': jax.random.randint(ks[10], (B,), 0, DIM1), 'wf2': jax.random.randint(ks[11], (B,), 0, DIM2)}
        dims = [DEEP_IN] + HID + [1]
        for i in range(4):
            fan_in = dims[i]
            inp[f'W{i + 1}'] = jax.random.normal(ks[12 + i], (dims[i], dims[i + 1]), jnp.float32) / np.sqrt(fan_in)
            inp[f'b{i + 1}'] = jnp.zeros((dims[i + 1],), jnp.float32)
        for i in range(3):
            inp[f'g{i + 1}'] = jnp.ones((HID[i],), jnp.float32)
            inp[f'be{i + 1}'] = jnp.zeros((HID[i],), jnp.float32)
        return inp
    _L0_rec_all = _L0_rec_setup()
    _L0_rec_in = {k: v for k, v in _L0_rec_all.items() if k in ('item_emb', 'cat_emb', 'wide_emb1', 'wide_emb2', 'cross_W', 'W1', 'b1', 'W2', 'b2', 'W3', 'b3', 'W4', 'b4', 'g1', 'be1', 'g2', 'be2', 'g3', 'be3')}
    del _L0_rec_all
    return {'r_user_embeddings': r_user_embeddings, 'r_price_features': r_price_features, 'r_temporal_features': r_temporal_features, 'r_item_ids': r_item_ids, 'r_category_ids': r_category_ids, 'r_wf1': r_wf1, 'r_wf2': r_wf2, 'L0_rec_item_emb': _L0_rec_in['item_emb'], 'L0_rec_cat_emb': _L0_rec_in['cat_emb'], 'L0_rec_wide_emb1': _L0_rec_in['wide_emb1'], 'L0_rec_wide_emb2': _L0_rec_in['wide_emb2'], 'L0_rec_cross_W': _L0_rec_in['cross_W'], 'L0_rec_W1': _L0_rec_in['W1'], 'L0_rec_b1': _L0_rec_in['b1'], 'L0_rec_W2': _L0_rec_in['W2'], 'L0_rec_b2': _L0_rec_in['b2'], 'L0_rec_W3': _L0_rec_in['W3'], 'L0_rec_b3': _L0_rec_in['b3'], 'L0_rec_W4': _L0_rec_in['W4'], 'L0_rec_b4': _L0_rec_in['b4'], 'L0_rec_g1': _L0_rec_in['g1'], 'L0_rec_be1': _L0_rec_in['be1'], 'L0_rec_g2': _L0_rec_in['g2'], 'L0_rec_be2': _L0_rec_in['be2'], 'L0_rec_g3': _L0_rec_in['g3'], 'L0_rec_be3': _L0_rec_in['be3']}

def reference(r_user_embeddings, r_price_features, r_temporal_features, r_item_ids, r_category_ids, r_wf1, r_wf2, L0_rec_item_emb, L0_rec_cat_emb, L0_rec_wide_emb1, L0_rec_wide_emb2, L0_rec_cross_W, L0_rec_W1, L0_rec_b1, L0_rec_W2, L0_rec_b2, L0_rec_W3, L0_rec_b3, L0_rec_W4, L0_rec_b4, L0_rec_g1, L0_rec_be1, L0_rec_g2, L0_rec_be2, L0_rec_g3, L0_rec_be3):
    import jax
    import jax.numpy as jnp

    def _L0_rec_ref(user_embeddings, price_features, temporal_features, item_emb, cat_emb, wide_emb1, wide_emb2, cross_W, W1, b1, W2, b2, W3, b3, W4, b4, g1, be1, g2, be2, g3, be3, item_ids, category_ids, wf1, wf2):
        import jax, jax.numpy as jnp
        import numpy as np
        B = 2048
        NUM_ITEMS = 125000
        NUM_CATS = 1001
        USER_DIM = 64
        ITEM_DIM = 64
        CAT_DIM = 32
        DIM1 = 1250
        DIM2 = 1250
        DEEP_IN = USER_DIM + ITEM_DIM + CAT_DIM + 2 + 2
        HID = [128, 64, 32]
        BN_EPS = 1e-05

        def _bn(x, g, b):
            return x * (g / jnp.sqrt(1.0 + BN_EPS)) + b
        x = jnp.concatenate([user_embeddings, item_emb[item_ids], cat_emb[category_ids], price_features, temporal_features], axis=-1)
        x = jax.nn.relu(_bn(x @ W1 + b1, g1, be1))
        x = jax.nn.relu(_bn(x @ W2 + b2, g2, be2))
        x = jax.nn.relu(_bn(x @ W3 + b3, g3, be3))
        deep_out = x @ W4 + b4
        wide_out = wide_emb1[wf1] + wide_emb2[wf2]
        flat_idx = wf1 * DIM2 + wf2
        wide_out = wide_out + cross_W[flat_idx][:, None]
        return wide_out + deep_out
    y = _L0_rec_ref(r_user_embeddings, r_price_features, r_temporal_features, L0_rec_item_emb, L0_rec_cat_emb, L0_rec_wide_emb1, L0_rec_wide_emb2, L0_rec_cross_W, L0_rec_W1, L0_rec_b1, L0_rec_W2, L0_rec_b2, L0_rec_W3, L0_rec_b3, L0_rec_W4, L0_rec_b4, L0_rec_g1, L0_rec_be1, L0_rec_g2, L0_rec_be2, L0_rec_g3, L0_rec_be3, r_item_ids, r_category_ids, r_wf1, r_wf2)
    return y

_drawn_inputs = setup_inputs


def setup_inputs(seed=0):
    import zlib

    import numpy as np

    out = dict(_drawn_inputs(seed))
    spreads = {'L0_rec_b1': (0.0, 0.1),
     'L0_rec_b2': (0.0, 0.1),
     'L0_rec_b3': (0.0, 0.1),
     'L0_rec_g1': (1.0, 0.2),
     'L0_rec_be1': (0.0, 0.1),
     'L0_rec_g2': (1.0, 0.2),
     'L0_rec_be2': (0.0, 0.1),
     'L0_rec_g3': (1.0, 0.2),
     'L0_rec_be3': (0.0, 0.1)}
    factors = {'L0_rec_item_emb': 3.383, 'L0_rec_cat_emb': 4.137, 'L0_rec_cross_W': 8.0}
    for name, (base, spread) in spreads.items():
        noise = np.random.default_rng([zlib.crc32(name.encode()), seed]).standard_normal(out[name].shape)
        drawn = base * np.exp(spread * noise) if base else spread * noise
        out[name] = jnp.asarray(drawn.astype(out[name].dtype))
    for name, factor in factors.items():
        out[name] = (out[name] * factor).astype(out[name].dtype)
    return out
```

```python
import concourse.bass as bass
from concourse import mybir
from contextlib import ExitStack

P = 128
B = 512
TILES = B // P
USER, ITEM, CAT, PRICE, TIME = 64, 64, 32, 2, 2
ITEMS, CATS, DIM1, DIM2 = 125000, 1001, 1250, 1250
H1, H2, H3 = 128, 64, 32
BN_EPS = 1e-05
BN_SCALE = (1.0 + BN_EPS) ** -0.5

DIRECT = USER + PRICE + TIME
PARTS = 3
CHUNKS = -(-CATS // P)
LO = 32
LO_BITS = LO.bit_length() - 1
HALF = P // 2
WIDE = 2

W1A, W1B, W1C = 0, H1, 2 * H1
W2C = 3 * H1
W3C = W2C + H2
W4C = W3C + H3
GAIN = W4C + 1
BIAS_COL = GAIN + H1 + H2 + H3
GAIN_COL, BETA_COL = BIAS_COL + 3, BIAS_COL + 6
PACKED = BIAS_COL + 9
TABLES = CHUNKS * CAT + WIDE * LO
SIZE_C, LAST_C, SHIFT_C, START_C = P, P + 1, P + 2, P + 3
ROW_COLS = P + 4
ROWS = 3 * TILES


def wide_deep_kernel(nc, id_cols, id_rows, features, tables, packed, item_emb, cross_w, out):
    f32, bf16, f16, i32 = mybir.dt.float32, mybir.dt.bfloat16, mybir.dt.float16, mybir.dt.int32
    ALU, ACT, AX = mybir.AluOpType, mybir.ActivationFunctionType, mybir.AxisListType

    ctx = ExitStack()
    with ctx:
        def sb(name, shape, dt):
            return ctx.enter_context(nc.sbuf_tensor(name, shape, dt))

        def sem(name):
            return ctx.enter_context(nc.semaphore(name))

        idc = sb("idc", [P, 3 * TILES], i32)
        idr = sb("idr", [ROWS, ROW_COLS], i32)
        xa = sb("xa", [DIRECT, B], f32)
        tab = sb("tab", [P, TABLES], f32)
        w = sb("w", [P, PACKED], f32)
        item_rows = sb("item_rows", [P, TILES, ITEM], f32)
        cross = sb("cross", [P, TILES], f32)
        ident = sb("ident", [P, P], f32)
        ident16 = sb("ident16", [ROWS, ROWS], f16)
        chunk_row = sb("chunk_row", [P, CHUNKS], f32)
        lo_iota = sb("lo_iota", [P, LO], i32)
        sizes = sb("sizes", [P, 3 * TILES], f32)
        lasts = sb("lasts", [P, 3 * TILES], f32)
        dim2 = sb("dim2", [P, TILES], i32)
        wrap = sb("wrap", [P, 3 * TILES], f32)
        wrapped = sb("wrapped", [P, 3 * TILES], f32)
        index = sb("index", [P, 3 * TILES], i32)
        lo_index = sb("lo_index", [P, 2 * TILES], i32)
        flat_product = sb("flat_product", [P, TILES], i32)
        flat = sb("flat", [P, TILES], i32)
        flat_wrap = sb("flat_wrap", [P, TILES], f32)
        flat_wrapped = sb("flat_wrapped", [P, TILES], f32)
        flat_index = sb("flat_index", [P, TILES], i32)
        row_wrap = sb("row_wrap", [ROWS, P], f32)
        row_wrapped = sb("row_wrapped", [ROWS, P], f32)
        row_index = sb("row_index", [ROWS, P], i32)
        row_hi = sb("row_hi", [ROWS, P], i32)
        row16 = sb("row16", [ROWS, P], f16)
        cat_ids = sb("cat_ids", [P, B], f16)
        cat_hot = sb("cat_hot", [P, CHUNKS, B], bf16)
        hi_hot = sb("hi_hot", [P, B], f32)
        lo_hot = sb("lo_hot", [P, WIDE * TILES, LO], f32)
        cat_parts = sb("cat_parts", [P, CHUNKS, PARTS, CAT], bf16)
        rest1 = sb("rest1", [P, CHUNKS, CAT], f32)
        rest2 = sb("rest2", [P, CHUNKS, CAT], f32)
        picked = sb("picked", [P, TILES, WIDE * LO], f32)
        wide = sb("wide", [P, TILES], f32)
        wf = sb("wf", [P, W4C], f32)
        gain_bias = sb("gain_bias", [P, 3], f32)
        shift = sb("shift", [P, 3], f32)
        xb = sb("xb", [PARTS * CAT, B], f32)
        xc = sb("xc", [ITEM, B], f32)
        h1 = sb("h1", [H1, B], f32)
        h2 = sb("h2", [H2, B], f32)
        h3 = sb("h3", [H3 + 1, B], f32)
        act_warm = sb("act_warm", [P, 1], f32)
        deep_wide = sb("deep_wide", [P, TILES], f32)
        total = sb("total", [P, TILES], f32)

        bank = [ctx.enter_context(nc.psum_tensor(f"bank{i}", [P, 512], f32)) for i in range(8)]
        cat_bc, hi_bc, cat_ps, wide_ps = bank[0], bank[1], bank[2], bank[3]
        h1_ps = [bank[4], bank[5]]
        item_ps = [bank[6], bank[7]]
        h2_ps = [bank[0], bank[1]]
        h3_ps = [bank[2], bank[3]]
        deep_ps = bank[6]

        def blk(t):
            return slice((t // 2) * P, (t // 2 + 1) * P)

        def cols(t):
            return slice(t * P, (t + 1) * P)

        s_idc, s_idr, s_xa, s_tab, s_w = (sem(n) for n in ("s_idc", "s_idr", "s_xa", "s_tab", "s_w"))
        s_item = [sem(f"s_item{t}") for t in range(TILES)]
        s_cross = sem("s_cross")
        s_out = sem("s_out")
        ident0 = sem("ident0")
        ident_ready = sem("ident_ready")
        dim2_ready = sem("dim2_ready")
        iota_ready = sem("iota_ready")
        const_ready = sem("const_ready")
        ident16_ready = sem("ident16_ready")
        wrap_done, wrapped_done, index_ready = sem("wrap_done"), sem("wrapped_done"), sem("index_ready")
        lo_index_done = sem("lo_index_done")
        product_done, flat_ready = sem("product_done"), sem("flat_ready")
        flat_wrap_done, flat_wrapped_done, flat_index_ready = sem("flat_wrap_done"), sem("flat_wrapped_done"), sem("flat_index_ready")
        row_step = sem("row_step")
        row16_ready = sem("row16_ready")
        cat_bc_ready, hi_bc_ready = sem("cat_bc_ready"), sem("hi_bc_ready")
        cat_ids_ready, cat_hot_ready, hi_hot_ready = sem("cat_ids_ready"), sem("cat_hot_ready"), sem("hi_hot_ready")
        part_hi_done, rest1_done, part_mid_done, part_lo_done = sem("part_hi_done"), sem("rest1_done"), sem("part_mid_done"), sem("part_lo_done")
        lo_hot_ready, wide_ps_ready, picked_done, wide_ready = sem("lo_hot_ready"), sem("wide_ps_ready"), sem("picked_done"), sem("wide_ready")
        wf_ready, gain_bias_done, shift_ready = sem("wf_ready"), sem("gain_bias_done"), sem("shift_ready")
        cat_ps_ready, xb_ready = sem("cat_ps_ready"), sem("xb_ready")
        item_ps_ready, xc_ready = sem("item_ps_ready"), sem("xc_ready")
        h1_ps_ready, h1_ready = sem("h1_ps_ready"), sem("h1_ready")
        h2_ps_ready, h2_ready = sem("h2_ps_ready"), sem("h2_ready")
        h3_ps_ready, h3_ready = sem("h3_ps_ready"), sem("h3_ready")
        ones_ready = sem("ones_ready")
        deep_ready, deep_wide_done, total_ready = sem("deep_ready"), sem("deep_wide_done"), sem("total_ready")

        block = ctx.enter_context(nc.Block())

        @block.sync
        def _(sp):
            sp.dma_start(idc[:, :], id_cols).then_inc(s_idc, 16)
            sp.dma_start(xa[:, :], features).then_inc(s_xa, 16)
            sp.wait_ge(total_ready, 1)
            sp.dma_start(out, total[:, :]).then_inc(s_out, 16)
            sp.wait_ge(s_out, 16)

        @block.gpsimd
        def _(pool):
            pool.memset(dim2[:, :], DIM2).then_inc(dim2_ready, 1)
            pool.memset(ident[:, :], 0.0).then_inc(ident0, 1)
            pool.iota(chunk_row[:, :], pattern=[[P, CHUNKS]], base=0, channel_multiplier=1,
                      allow_small_or_imprecise_dtypes=True).then_inc(iota_ready, 1)
            pool.iota(lo_iota[:, :], pattern=[[1, LO]], base=0, channel_multiplier=0).then_inc(iota_ready, 1)
            pool.wait_ge(ident0, 1)
            pool.affine_select(out=ident[:, :], in_=ident[:, :], compare_op=ALU.not_equal, fill=1.0,
                               base=0, pattern=[[-1, P]], channel_multiplier=1).then_inc(ident_ready, 1)
            pool.wait_ge(s_idc, 16)
            pool.wait_ge(dim2_ready, 1)
            pool.tensor_tensor(flat_product[:, :], idc[:, TILES:2 * TILES], dim2[:, :], ALU.mult)\
                .then_inc(product_done, 1)
            pool.wait_ge(product_done, 1)
            pool.tensor_tensor(flat[:, :], flat_product[:, :], idc[:, 2 * TILES:], ALU.add).then_inc(flat_ready, 1)
            pool.wait_ge(index_ready, 1)
            for t in range(TILES):
                pool.indirect_dma_start(item_rows[:, t, :], None, item_emb,
                                        bass.IndirectOffsetOnAxis(index[:, t:t + 1], 0)).then_inc(s_item[t], 16)
            pool.wait_ge(flat_index_ready, 1)
            for t in range(TILES):
                pool.indirect_dma_start(cross[:, t:t + 1], None, cross_w,
                                        bass.IndirectOffsetOnAxis(flat_index[:, t:t + 1], 0)).then_inc(s_cross, 16)

        @block.scalar
        def _(act):
            act.dma_start(idr[:, :], id_rows).then_inc(s_idr, 16)
            act.dma_start(tab[:, :], tables).then_inc(s_tab, 16)
            act.dma_start(w[:, :], packed).then_inc(s_w, 16)
            cat_tab = tab[:, 0:CHUNKS * CAT].rearrange("p (k d) -> p k d", d=CAT)
            act.wait_ge(s_tab, 16)
            nc.scalar.activation(cat_parts[:, :, 0, :], cat_tab, ACT.Copy).then_inc(part_hi_done, 1)
            act.wait_ge(cat_bc_ready, 1)
            nc.scalar.activation(cat_ids[:, :], cat_bc[:, :], ACT.Copy).then_inc(cat_ids_ready, 1)
            act.wait_ge(rest1_done, 1)
            nc.scalar.activation(cat_parts[:, :, 1, :], rest1[:, :, :], ACT.Copy).then_inc(part_mid_done, 1)
            act.wait_ge(cat_ps_ready, 1)
            nc.scalar.activation(xb[:, :], cat_ps[0:PARTS * CAT, :], ACT.Copy).then_inc(xb_ready, 1)
            for t in range(TILES):
                act.wait_ge(item_ps_ready, t + 1)
                nc.scalar.activation(xc[:, cols(t)], item_ps[t % 2][0:ITEM, blk(t)], ACT.Copy).then_inc(xc_ready, 1)

        @block.vector
        def _(dve):
            nc.vector.memset(sizes[:, 0:TILES], float(ITEMS))
            nc.vector.memset(sizes[:, TILES:], float(DIM1))
            nc.vector.memset(lasts[:, 0:TILES], float(ITEMS - 1))
            nc.vector.memset(lasts[:, TILES:], float(DIM1 - 1)).then_inc(const_ready, 1)
            nc.vector.memset(h3[H3:H3 + 1, :], 1.0).then_inc(ones_ready, 1)
            dve.wait_ge(ident_ready, 1)
            nc.vector.tensor_copy(ident16[:, :], ident[0:ROWS, 0:ROWS]).then_inc(ident16_ready, 1)

            dve.wait_ge(const_ready, 1)
            dve.wait_ge(s_idc, 16)
            nc.vector.scalar_tensor_tensor(wrap[:, :], idc[:, :], 0.0, sizes[:, :], ALU.is_lt, ALU.mult)\
                .then_inc(wrap_done, 1)
            dve.wait_ge(wrap_done, 1)
            nc.vector.tensor_tensor(wrapped[:, :], wrap[:, :], idc[:, :], ALU.add).then_inc(wrapped_done, 1)
            dve.wait_ge(wrapped_done, 1)
            nc.vector.scalar_tensor_tensor(index[:, :], wrapped[:, :], 0.0, lasts[:, :], ALU.max, ALU.min)\
                .then_inc(index_ready, 1)

            dve.wait_ge(s_idr, 16)
            nc.vector.tensor_scalar(row_wrap[:, :], idr[:, 0:P], 0.0, idr[:, SIZE_C:SIZE_C + 1],
                                    ALU.is_lt, ALU.mult).then_inc(row_step, 1)
            dve.wait_ge(row_step, 1)
            nc.vector.tensor_tensor(row_wrapped[:, :], row_wrap[:, :], idr[:, 0:P], ALU.add).then_inc(row_step, 1)
            dve.wait_ge(row_step, 2)
            nc.vector.tensor_scalar(row_index[:, :], row_wrapped[:, :], 0.0, idr[:, LAST_C:LAST_C + 1],
                                    ALU.max, ALU.min).then_inc(row_step, 1)
            dve.wait_ge(row_step, 3)
            nc.vector.tensor_scalar(row_hi[:, :], row_index[:, :], idr[:, SHIFT_C:SHIFT_C + 1], None,
                                    ALU.logical_shift_right).then_inc(row_step, 1)
            dve.wait_ge(row_step, 4)
            nc.vector.tensor_scalar(row16[:, :], row_hi[:, :], idr[:, START_C:START_C + 1], None, ALU.add)\
                .then_inc(row16_ready, 1)

            dve.wait_ge(flat_ready, 1)
            nc.vector.tensor_scalar(flat_wrap[:, :], flat[:, :], 0.0, float(DIM1 * DIM2), ALU.is_lt, ALU.mult)\
                .then_inc(flat_wrap_done, 1)
            dve.wait_ge(flat_wrap_done, 1)
            nc.vector.tensor_tensor(flat_wrapped[:, :], flat_wrap[:, :], flat[:, :], ALU.add)\
                .then_inc(flat_wrapped_done, 1)
            dve.wait_ge(flat_wrapped_done, 1)
            nc.vector.tensor_scalar(flat_index[:, :], flat_wrapped[:, :], 0.0, float(DIM1 * DIM2 - 1),
                                    ALU.max, ALU.min).then_inc(flat_index_ready, 1)

            cat_tab = tab[:, 0:CHUNKS * CAT].rearrange("p (k d) -> p k d", d=CAT)
            dve.wait_ge(s_tab, 16)
            dve.wait_ge(part_hi_done, 1)
            nc.vector.tensor_tensor(rest1[:, :, :], cat_tab, cat_parts[:, :, 0, :], ALU.subtract)\
                .then_inc(rest1_done, 1)

            dve.wait_ge(iota_ready, 2)
            dve.wait_ge(hi_bc_ready, 1)
            nc.vector.tensor_scalar(hi_hot[:, :], hi_bc[:, :], chunk_row[:, 0:1], None, ALU.is_equal)\
                .then_inc(hi_hot_ready, 1)

            dve.wait_ge(s_w, 16)
            nc.vector.scalar_tensor_tensor(
                wf[:, 0:3 * H1].rearrange("p (a n) -> p a n", a=3), w[:, 0:3 * H1].rearrange("p (a n) -> p a n", a=3),
                BN_SCALE, w[:, GAIN:GAIN + H1].unsqueeze(1).to_broadcast([P, 3, H1]), ALU.mult, ALU.mult)\
                .then_inc(wf_ready, 1)

            dve.wait_ge(cat_ids_ready, 1)
            for k in range(CHUNKS):
                nc.vector.tensor_scalar(cat_hot[:, k, :], cat_ids[:, :], chunk_row[:, k:k + 1], None, ALU.is_equal)\
                    .then_inc(cat_hot_ready, 1)
                if k == 0:
                    dve.wait_ge(rest1_done, 1)
                    dve.wait_ge(part_mid_done, 1)
                    nc.vector.tensor_tensor(cat_parts[:, :, 2, :], rest1[:, :, :], cat_parts[:, :, 1, :],
                                            ALU.subtract).then_inc(part_lo_done, 1)

            nc.vector.scalar_tensor_tensor(wf[:, W2C:W4C], w[:, W2C:W4C], BN_SCALE,
                                           w[:, GAIN + H1:GAIN + H1 + H2 + H3], ALU.mult, ALU.mult)\
                .then_inc(wf_ready, 1)
            nc.vector.scalar_tensor_tensor(gain_bias[:, :], w[:, GAIN_COL:GAIN_COL + 3], BN_SCALE,
                                           w[:, BIAS_COL:BIAS_COL + 3], ALU.mult, ALU.mult)\
                .then_inc(gain_bias_done, 1)
            dve.wait_ge(gain_bias_done, 1)
            nc.vector.tensor_tensor(shift[:, :], gain_bias[:, :], w[:, BETA_COL:BETA_COL + 3], ALU.add)\
                .then_inc(shift_ready, 1)

            def wide_lo():
                dve.wait_ge(index_ready, 1)
                nc.vector.tensor_scalar(lo_index[:, :], index[:, TILES:], LO - 1, None, ALU.bitwise_and)\
                    .then_inc(lo_index_done, 1)
                dve.wait_ge(lo_index_done, 1)
                nc.vector.tensor_tensor(lo_hot[:, :, :],
                                        lo_index[:, :].unsqueeze(2).to_broadcast([P, WIDE * TILES, LO]),
                                        lo_iota[:, :].unsqueeze(1).to_broadcast([P, WIDE * TILES, LO]),
                                        ALU.is_equal).then_inc(lo_hot_ready, 1)

            def wide_pick():
                dve.wait_ge(lo_hot_ready, 1)
                dve.wait_ge(wide_ps_ready, 1)
                hot = lo_hot[:, :, :].rearrange("p (a t) l -> p t a l", a=WIDE)
                nc.vector.tensor_tensor(picked[:, :, :].rearrange("p t (a l) -> p t a l", a=WIDE),
                                        wide_ps[:, 0:TILES * WIDE * LO].rearrange("p (t a l) -> p t a l", t=TILES, a=WIDE),
                                        hot, ALU.mult).then_inc(picked_done, 1)
                dve.wait_ge(picked_done, 1)
                nc.vector.tensor_reduce(wide[:, :], picked[:, :, :], AX.X, ALU.add).then_inc(wide_ready, 1)

            wide_lo()
            wide_pick()

            dve.wait_ge(shift_ready, 1)

            def relu(dst, src, n, layer, ready, done, t):
                dve.wait_ge(ready, t + 1)
                nc.vector.tensor_scalar(dst[0:n, cols(t)], src[t % 2][0:n, blk(t)], shift[0:n, layer:layer + 1], 0.0,
                                        ALU.add, ALU.max).then_inc(done, 1)

            for s in range(TILES + 2):
                if s >= 2:
                    relu(h3, h3_ps, H3, 2, h3_ps_ready, h3_ready, s - 2)
                if 1 <= s <= TILES:
                    relu(h2, h2_ps, H2, 1, h2_ps_ready, h2_ready, s - 1)
                if s < TILES:
                    relu(h1, h1_ps, H1, 0, h1_ps_ready, h1_ready, s)

            dve.wait_ge(wide_ready, 1)
            dve.wait_ge(deep_ready, 1)
            nc.vector.tensor_tensor(deep_wide[:, :], deep_ps[:, 0:TILES], wide[:, :], ALU.add)\
                .then_inc(deep_wide_done, 1)
            dve.wait_ge(deep_wide_done, 1)
            dve.wait_ge(s_cross, 16 * TILES)
            nc.vector.tensor_tensor(total[:, :], deep_wide[:, :], cross[:, :], ALU.add).then_inc(total_ready, 1)

        @block.tensor
        def _(pe):
            pe.wait_ge(ident16_ready, 1)
            pe.wait_ge(row16_ready, 1)
            for t in range(TILES):
                last = nc.tensor.matmul(cat_bc[:, cols(t)], ident16[:, t:t + 1].to_broadcast([ROWS, P]),
                                        row16[:, :], start=True, stop=True)
            last.then_inc(cat_bc_ready, 1)
            for a in range(WIDE):
                for t in range(TILES):
                    row = (a + 1) * TILES + t
                    last = nc.tensor.matmul(hi_bc[a * HALF:(a + 1) * HALF, cols(t)],
                                            ident16[:, row:row + 1].to_broadcast([ROWS, HALF]),
                                            row16[:, :], start=True, stop=True)
            last.then_inc(hi_bc_ready, 1)

            wide_tab = tab[:, CHUNKS * CAT:TABLES]
            pe.wait_ge(s_tab, 16)
            pe.wait_ge(hi_hot_ready, 1)
            for t in range(TILES):
                last = nc.tensor.matmul(wide_ps[:, t * WIDE * LO:(t + 1) * WIDE * LO], hi_hot[:, cols(t)], wide_tab,
                                        start=True, stop=True)
            last.then_inc(wide_ps_ready, 1)

            pe.wait_ge(s_xa, 16)
            pe.wait_ge(wf_ready, 1)
            for e in range(2):
                rhs = xa[:, :].rearrange("p (b e n) -> p e b n", e=2, n=P)[:, e, :, :]
                nc.tensor.matmul(h1_ps[e][:, 0:2 * P], wf[0:DIRECT, W1A:W1A + H1], rhs,
                                 start=True, stop=False, skip_group_check=True)

            pe.wait_ge(part_hi_done, 1)
            pe.wait_ge(part_mid_done, 1)
            pe.wait_ge(part_lo_done, 1)
            for k in range(CHUNKS):
                pe.wait_ge(cat_hot_ready, k + 1)
                last = nc.tensor.matmul(cat_ps[0:PARTS * CAT, :], cat_parts[:, k, :, :], cat_hot[:, k, :],
                                        start=(k == 0), stop=(k == CHUNKS - 1))
            last.then_inc(cat_ps_ready, 1)

            pe.wait_ge(xb_ready, 1)
            for e in range(2):
                rhs = xb[:, :].rearrange("p (b e n) -> p e b n", e=2, n=P)[:, e, :, :]
                nc.tensor.matmul(h1_ps[e][:, 0:2 * P], wf[0:PARTS * CAT, W1B:W1B + H1], rhs,
                                 start=False, stop=False, skip_group_check=True)

            def transpose(t):
                pe.wait_ge(ident_ready, 1)
                pe.wait_ge(s_item[t], 16)
                if t >= 2:
                    pe.wait_ge(xc_ready, t - 1)
                nc.tensor.transpose(item_ps[t % 2][0:ITEM, blk(t)], item_rows[:, t, :], ident[:, :])\
                    .then_inc(item_ps_ready, 1)

            def layer1(t):
                pe.wait_ge(xc_ready, t + 1)
                if t >= 2:
                    pe.wait_ge(h1_ready, t - 1)
                nc.tensor.matmul(h1_ps[t % 2][:, blk(t)], wf[0:ITEM, W1C:W1C + H1], xc[:, cols(t)],
                                 start=False, stop=True, skip_group_check=True).then_inc(h1_ps_ready, 1)

            def layer2(t):
                pe.wait_ge(wf_ready, 2)
                pe.wait_ge(h1_ready, t + 1)
                if t >= 2:
                    pe.wait_ge(h2_ready, t - 1)
                nc.tensor.matmul(h2_ps[t % 2][0:H2, blk(t)], wf[:, W2C:W2C + H2], h1[:, cols(t)],
                                 start=True, stop=True).then_inc(h2_ps_ready, 1)

            def layer3(t):
                pe.wait_ge(h2_ready, t + 1)
                pe.wait_ge(picked_done, 1)
                if t >= 2:
                    pe.wait_ge(h3_ready, t - 1)
                nc.tensor.matmul(h3_ps[t % 2][0:H3, blk(t)], wf[0:H2, W3C:W3C + H3], h2[:, cols(t)],
                                 start=True, stop=True).then_inc(h3_ps_ready, 1)

            for s in range(TILES + 2):
                if s < TILES:
                    transpose(s)
                if s >= 2:
                    layer3(s - 2)
                if 1 <= s <= TILES:
                    layer2(s - 1)
                if s < TILES:
                    layer1(s)

            pe.wait_ge(s_w, 16)
            pe.wait_ge(ones_ready, 1)
            for t in range(TILES):
                pe.wait_ge(h3_ready, t + 1)
                last = nc.tensor.matmul(deep_ps[:, t:t + 1], h3[:, cols(t)], w[0:H3 + 1, W4C:W4C + 1],
                                        start=True, stop=True)
            last.then_inc(deep_ready, 1)


def kernel(**inputs):
    import numpy as np
    import concourse.bacc as bacc
    from concourse.bass_utils import run_bass_kernel_spmd

    g = {k.replace("L0_rec_", ""): np.asarray(v) for k, v in inputs.items()}

    def tiles(ids):
        return ids.reshape(TILES, P)

    def rows(a, n=P):
        return np.pad(a, ((0, n - a.shape[0]), (0, 0)))

    id_cols = np.concatenate([tiles(g[k]).T for k in ("r_item_ids", "r_wf1", "r_wf2")], axis=1)
    size = np.repeat(np.array([CATS, DIM1, DIM2], np.int32), TILES)
    last = np.repeat(np.array([CATS - 1, DIM1 - 1, DIM2 - 1], np.int32), TILES)
    cut = np.repeat(np.array([0, LO_BITS, LO_BITS], np.int32), TILES)
    start = np.repeat(np.array([0, 0, HALF], np.int32), TILES)
    id_rows = np.concatenate([np.concatenate([tiles(g[k]) for k in ("r_category_ids", "r_wf1", "r_wf2")], axis=0),
                              size[:, None], last[:, None], cut[:, None], start[:, None]], axis=1)
    features = np.concatenate([g["r_user_embeddings"].T, g["r_price_features"].T, g["r_temporal_features"].T], axis=0)

    cat = rows(g["cat_emb"], CHUNKS * P).reshape(CHUNKS, P, CAT).transpose(1, 0, 2).reshape(P, CHUNKS * CAT)
    wide = [rows(g[k], HALF * LO).reshape(HALF, LO) for k in ("wide_emb1", "wide_emb2")]
    blank = np.zeros((HALF, LO), np.float32)
    tables = np.concatenate([cat, np.block([[wide[0], blank], [blank, wide[1]]])], axis=1)

    w1 = g["W1"]
    w1_user, w1_item, w1_cat, w1_rest = np.split(w1, [USER, USER + ITEM, USER + ITEM + CAT])
    gains = np.concatenate([g["g1"], g["g2"], g["g3"]])
    columns = [rows(g[f"{k}{i}"][:, None]) for k in ("b", "g", "be") for i in (1, 2, 3)]
    packed = np.concatenate(
        [rows(np.concatenate([w1_user, w1_rest])), rows(np.concatenate([w1_cat] * PARTS)), rows(w1_item),
         rows(g["W2"]), rows(g["W3"]), rows(np.concatenate([g["W4"], g["b4"][None, :]])),
         np.broadcast_to(gains, (P, gains.shape[0]))] + columns, axis=1)

    arrays = {"id_cols": id_cols, "id_rows": id_rows, "features": features, "tables": tables, "packed": packed,
              "item_emb": g["item_emb"], "cross_w": g["cross_W"].reshape(-1, 1)}
    arrays = {k: np.ascontiguousarray(v) for k, v in arrays.items()}

    nc = bacc.Bacc("TRN2", target_bir_lowering=False, num_devices=1)
    aps = [nc.dram_tensor(k, v.shape, mybir.dt.from_np(v.dtype), kind="ExternalInput").ap() for k, v in arrays.items()]
    out = nc.dram_tensor("out", (P, TILES), mybir.dt.float32, kind="ExternalOutput").ap()
    wide_deep_kernel(nc, *aps, out)
    r = run_bass_kernel_spmd(nc, [arrays], core_ids=[0])
    return r.results[0]["out"].T.reshape(B, 1)
```

```python
import concourse.bass as bass
from concourse import mybir
from contextlib import ExitStack

P = 128
B = 512
TILES = B // P
USER, ITEM, CAT, PRICE, TIME = 64, 64, 32, 2, 2
ITEMS, CATS, DIM1, DIM2 = 125000, 1001, 1250, 1250
H1, H2, H3 = 128, 64, 32
BN_EPS = 1e-05
BN_SCALE = (1.0 + BN_EPS) ** -0.5

PARTS = 3
CHUNKS = -(-CATS // P)
LO = 32
LO_BITS = LO.bit_length() - 1
HALF = P // 2
WIDE = 2

W1A, W1B = 0, H1
W2C = 2 * H1
W3C = W2C + H2
W4C = W3C + H3
GAIN = W4C + 1
BIAS_COL = GAIN + H1 + H2 + H3
GAIN_COL, BETA_COL = BIAS_COL + 3, BIAS_COL + 6
PACKED = BIAS_COL + 9
XA = ITEM + USER
XB = PARTS * CAT + PRICE + TIME
TABLES = CHUNKS * CAT + WIDE * LO
SIZE_C, LAST_C, SHIFT_C, START_C = P, P + 1, P + 2, P + 3
ROW_COLS = P + 4
ROWS = 3 * TILES
WARM_UP = 8


def wide_deep_kernel(nc, id_cols, id_rows, user, price_time, tables, packed, item_emb, cross_w, out):
    f32, bf16, f16, i32 = mybir.dt.float32, mybir.dt.bfloat16, mybir.dt.float16, mybir.dt.int32
    ALU, ACT, AX = mybir.AluOpType, mybir.ActivationFunctionType, mybir.AxisListType

    ctx = ExitStack()
    with ctx:
        def sb(name, shape, dt):
            return ctx.enter_context(nc.sbuf_tensor(name, shape, dt))

        def sem(name):
            return ctx.enter_context(nc.semaphore(name))

        idc = sb("idc", [P, 3 * TILES], i32)
        idr = sb("idr", [ROWS, ROW_COLS], i32)
        tab = sb("tab", [P, TABLES], f32)
        w = sb("w", [P, PACKED], f32)
        item_rows = sb("item_rows", [P, TILES, ITEM], f32)
        cross = sb("cross", [P, TILES], f32)
        blank = sb("blank", [P, P], bf16)
        ident = sb("ident", [P, P], f32)
        ident16 = sb("ident16", [ROWS, ROWS], f16)
        chunk_row = sb("chunk_row", [P, CHUNKS], f32)
        lo_iota = sb("lo_iota", [P, LO], i32)
        sizes = sb("sizes", [P, 3 * TILES], f32)
        lasts = sb("lasts", [P, 3 * TILES], f32)
        dim2 = sb("dim2", [P, TILES], i32)
        wrap = sb("wrap", [P, 3 * TILES], f32)
        wrapped = sb("wrapped", [P, 3 * TILES], f32)
        index = sb("index", [P, 3 * TILES], i32)
        lo_index = sb("lo_index", [P, 2 * TILES], i32)
        flat_product = sb("flat_product", [P, TILES], i32)
        flat = sb("flat", [P, TILES], i32)
        flat_wrap = sb("flat_wrap", [P, TILES], f32)
        flat_wrapped = sb("flat_wrapped", [P, TILES], f32)
        flat_index = sb("flat_index", [P, TILES], i32)
        row_wrap = sb("row_wrap", [ROWS, P], f32)
        row_wrapped = sb("row_wrapped", [ROWS, P], f32)
        row16 = sb("row16", [ROWS, P], f16)
        row_index = sb("row_index", [ROWS, P], i32)
        row_hi = sb("row_hi", [ROWS, P], i32)
        row_hi16 = sb("row_hi16", [ROWS, P], f16)
        cat_ids = sb("cat_ids", [P, B], f16)
        hi_ids = sb("hi_ids", [P, B], f16)
        cat_hot = sb("cat_hot", [P, CHUNKS, B], bf16)
        hi_hot = sb("hi_hot", [P, B], f32)
        lo_hot = sb("lo_hot", [P, WIDE * TILES, LO], f32)
        cat_parts = sb("cat_parts", [P, CHUNKS, PARTS, CAT], bf16)
        rest1 = sb("rest1", [P, CHUNKS, CAT], f32)
        picked = sb("picked", [P, TILES, WIDE * LO], f32)
        wide = sb("wide", [P, TILES], f32)
        wf = sb("wf", [P, W4C], f32)
        gain_bias = sb("gain_bias", [P, 3], f32)
        shift = sb("shift", [P, 3], f32)
        xa = sb("xa", [XA, B], f32)
        xb = sb("xb", [XB, B], f32)
        h1 = sb("h1", [H1, B], f32)
        h2 = sb("h2", [H2, B], f32)
        h3 = sb("h3", [H3 + 1, B], f32)
        table_loaded = sb("table_loaded", [1, 1], f32)
        deep_wide = sb("deep_wide", [P, TILES], f32)
        total = sb("total", [P, TILES], f32)

        bank = [ctx.enter_context(nc.psum_tensor(f"bank{i}", [P, 512], f32)) for i in range(8)]
        cat_bc, hi_bc, cat_ps, wide_ps = bank[0], bank[1], bank[2], bank[3]
        h1_ps = [bank[4], bank[5]]
        item_ps = [bank[6], bank[7]]
        h2_ps = [bank[0], bank[1]]
        h3_ps = [bank[2], bank[3]]
        deep_ps = bank[6]
        warm_ps = bank[7]

        def blk(t):
            return slice((t // 2) * P, (t // 2 + 1) * P)

        def cols(t):
            return slice(t * P, (t + 1) * P)

        def parity(x, e):
            return x.rearrange("p (b e n) -> p e b n", e=2, n=P)[:, e, :, :]

        s_idc, s_idr, s_user, s_price, s_tab, s_w = (sem(f"loaded_{n}") for n in ("idc", "idr", "user", "price", "tab", "w"))
        s_item = [sem(f"s_item{t}") for t in range(TILES)]
        s_cross, s_out = sem("s_cross"), sem("s_out")
        blank_ready, ident0, ident_ready, ident16_ready = sem("blank_ready"), sem("ident0"), sem("ident_ready"), sem("ident16_ready")
        dim2_ready, iota_ready, const_ready, ones_ready = sem("dim2_ready"), sem("iota_ready"), sem("const_ready"), sem("ones_ready")
        wrap_done, wrapped_done, index_ready = sem("wrap_done"), sem("wrapped_done"), sem("index_ready")
        lo_index_done, lo_hot_ready = sem("lo_index_done"), sem("lo_hot_ready")
        product_done, flat_ready = sem("product_done"), sem("flat_ready")
        flat_wrap_done, flat_wrapped_done, flat_index_ready = sem("flat_wrap_done"), sem("flat_wrapped_done"), sem("flat_index_ready")
        row_wrap_done, row_wrapped_done, row16_ready = sem("row_wrap_done"), sem("row_wrapped_done"), sem("row16_ready")
        row_index_done, row_hi_done, row_hi16_ready = sem("row_index_done"), sem("row_hi_done"), sem("row_hi16_ready")
        cat_bc_ready, hi_bc_ready, cat_ids_ready, hi_ids_ready = sem("cat_bc_ready"), sem("hi_bc_ready"), sem("cat_ids_ready"), sem("hi_ids_ready")
        cat_hot_ready, hi_hot_ready = sem("cat_hot_ready"), sem("hi_hot_ready")
        part_hi_done, rest1_done, part_mid_done, part_lo_done = sem("part_hi_done"), sem("rest1_done"), sem("part_mid_done"), sem("part_lo_done")
        wide_ps_ready, picked_done, wide_ready = sem("wide_ps_ready"), sem("picked_done"), sem("wide_ready")
        wf1_ready, wf23_ready, gain_bias_done, shift_ready = sem("wf1_ready"), sem("wf23_ready"), sem("gain_bias_done"), sem("shift_ready")
        cat_ps_ready, xb_ready = sem("cat_ps_ready"), sem("xb_ready")
        deep_ready, deep_wide_done, total_ready = sem("deep_ready"), sem("deep_wide_done"), sem("total_ready")
        item_ps_ready, item_ready = [sem(f"item_ps_ready{e}") for e in range(2)], [sem(f"item_ready{e}") for e in range(2)]
        h_ps_ready = [[sem(f"h{n}_ps_ready{e}") for e in range(2)] for n in (1, 2, 3)]
        h_ready = [[sem(f"h{n}_ready{e}") for e in range(2)] for n in (1, 2, 3)]
        layers = [(h1, h1_ps, H1), (h2, h2_ps, H2), (h3, h3_ps, H3)]

        block = ctx.enter_context(nc.Block())

        @block.sync
        def _(sp):
            sp.dma_start(idc[:, :], id_cols).then_inc(s_idc, 16)
            sp.dma_start(idr[:, :], id_rows).then_inc(s_idr, 16)
            sp.dma_start(w[:, :], packed).then_inc(s_w, 16)
            sp.dma_start(xb[PARTS * CAT:XB, :], price_time).then_inc(s_price, 16)
            sp.dma_start(xa[ITEM:XA, :], user).then_inc(s_user, 16)
            sp.wait_ge(total_ready, 1)
            sp.dma_start(out, total[:, :]).then_inc(s_out, 16)
            sp.wait_ge(s_out, 16)

        @block.gpsimd
        def _(pool):
            pool.dma_start(tab[:, :], tables).then_inc(s_tab, 16)
            pool.memset(dim2[:, :], DIM2).then_inc(dim2_ready, 1)
            pool.memset(ident[:, :], 0.0).then_inc(ident0, 1)
            pool.iota(chunk_row[:, :], pattern=[[P, CHUNKS]], base=0, channel_multiplier=1,
                      allow_small_or_imprecise_dtypes=True).then_inc(iota_ready, 1)
            pool.iota(lo_iota[:, :], pattern=[[1, LO]], base=0, channel_multiplier=0).then_inc(iota_ready, 1)
            pool.wait_ge(ident0, 1)
            pool.affine_select(out=ident[:, :], in_=ident[:, :], compare_op=ALU.not_equal, fill=1.0,
                               base=0, pattern=[[-1, P]], channel_multiplier=1).then_inc(ident_ready, 1)
            pool.wait_ge(s_idc, 16)
            pool.wait_ge(dim2_ready, 1)
            pool.tensor_tensor(flat_product[:, :], idc[:, TILES:2 * TILES], dim2[:, :], ALU.mult)\
                .then_inc(product_done, 1)
            pool.wait_ge(product_done, 1)
            pool.tensor_tensor(flat[:, :], flat_product[:, :], idc[:, 2 * TILES:], ALU.add).then_inc(flat_ready, 1)
            pool.wait_ge(index_ready, 1)
            for t in range(TILES):
                pool.indirect_dma_start(item_rows[:, t, :], None, item_emb,
                                        bass.IndirectOffsetOnAxis(index[:, t:t + 1], 0)).then_inc(s_item[t], 16)
            pool.wait_ge(flat_index_ready, 1)
            for t in range(TILES):
                pool.indirect_dma_start(cross[:, t:t + 1], None, cross_w,
                                        bass.IndirectOffsetOnAxis(flat_index[:, t:t + 1], 0)).then_inc(s_cross, 16)

        @block.scalar
        def _(act):
            act.wait_ge(blank_ready, 1)
            nc.scalar.activation(table_loaded[:, :], blank[0:1, 0:1], ACT.Relu)
            cat_tab = tab[:, 0:CHUNKS * CAT].rearrange("p (k d) -> p k d", d=CAT)
            act.wait_ge(s_tab, 16)
            nc.scalar.activation(cat_parts[:, :, 0, :], cat_tab, ACT.Copy).then_inc(part_hi_done, 1)
            act.wait_ge(rest1_done, 1)
            nc.scalar.activation(cat_parts[:, :, 1, :], rest1[:, :, :], ACT.Copy).then_inc(part_mid_done, 1)
            act.wait_ge(cat_bc_ready, 1)
            nc.scalar.activation(cat_ids[:, :], cat_bc[:, :], ACT.Copy).then_inc(cat_ids_ready, 1)
            act.wait_ge(hi_bc_ready, 1)
            nc.scalar.activation(hi_ids[:, :], hi_bc[:, :], ACT.Copy).then_inc(hi_ids_ready, 1)
            act.wait_ge(cat_ps_ready, 1)
            nc.scalar.activation(xb[0:PARTS * CAT, :], cat_ps[0:PARTS * CAT, :], ACT.Copy).then_inc(xb_ready, 1)

            for t in range(1, TILES, 2):
                act.wait_ge(item_ps_ready[1], t // 2 + 1)
                nc.scalar.activation(xa[0:ITEM, cols(t)], item_ps[1][0:ITEM, blk(t)], ACT.Copy)\
                    .then_inc(item_ready[1], 1)
            act.wait_ge(shift_ready, 1)
            for step in range(TILES // 2 + 2):
                for layer in (2, 1, 0):
                    t = 2 * (step - layer) + 1
                    if 0 <= t < TILES:
                        h, ps, n = layers[layer]
                        act.wait_ge(h_ps_ready[layer][1], t // 2 + 1)
                        nc.scalar.activation(h[0:n, cols(t)], ps[1][0:n, blk(t)], ACT.Relu,
                                             bias=shift[0:n, layer:layer + 1]).then_inc(h_ready[layer][1], 1)

        @block.vector
        def _(dve):
            nc.vector.memset(blank[:, :], 0.0).then_inc(blank_ready, 1)
            nc.vector.memset(sizes[:, 0:TILES], float(ITEMS))
            nc.vector.memset(sizes[:, TILES:], float(DIM1))
            nc.vector.memset(lasts[:, 0:TILES], float(ITEMS - 1))
            nc.vector.memset(lasts[:, TILES:], float(DIM1 - 1)).then_inc(const_ready, 1)
            nc.vector.memset(h3[H3:H3 + 1, :], 1.0).then_inc(ones_ready, 1)

            dve.wait_ge(const_ready, 1)
            dve.wait_ge(s_idc, 16)
            nc.vector.scalar_tensor_tensor(wrap[:, :], idc[:, :], 0.0, sizes[:, :], ALU.is_lt, ALU.mult)\
                .then_inc(wrap_done, 1)
            dve.wait_ge(wrap_done, 1)
            nc.vector.tensor_tensor(wrapped[:, :], wrap[:, :], idc[:, :], ALU.add).then_inc(wrapped_done, 1)
            dve.wait_ge(wrapped_done, 1)
            nc.vector.scalar_tensor_tensor(index[:, :], wrapped[:, :], 0.0, lasts[:, :], ALU.max, ALU.min)\
                .then_inc(index_ready, 1)

            dve.wait_ge(ident_ready, 1)
            nc.vector.tensor_copy(ident16[:, :], ident[0:ROWS, 0:ROWS]).then_inc(ident16_ready, 1)

            dve.wait_ge(s_idr, 16)
            nc.vector.tensor_scalar(row_wrap[:, :], idr[:, 0:P], 0.0, idr[:, SIZE_C:SIZE_C + 1],
                                    ALU.is_lt, ALU.mult).then_inc(row_wrap_done, 1)
            dve.wait_ge(flat_ready, 1)
            nc.vector.tensor_scalar(flat_wrap[:, :], flat[:, :], 0.0, float(DIM1 * DIM2), ALU.is_lt, ALU.mult)\
                .then_inc(flat_wrap_done, 1)
            dve.wait_ge(row_wrap_done, 1)
            nc.vector.tensor_tensor(row_wrapped[:, :], row_wrap[:, :], idr[:, 0:P], ALU.add)\
                .then_inc(row_wrapped_done, 1)
            dve.wait_ge(flat_wrap_done, 1)
            nc.vector.tensor_tensor(flat_wrapped[:, :], flat_wrap[:, :], flat[:, :], ALU.add)\
                .then_inc(flat_wrapped_done, 1)
            dve.wait_ge(row_wrapped_done, 1)
            nc.vector.tensor_scalar(row16[:, :], row_wrapped[:, :], 0.0, idr[:, LAST_C:LAST_C + 1],
                                    ALU.max, ALU.min).then_inc(row16_ready, 1)
            dve.wait_ge(flat_wrapped_done, 1)
            nc.vector.tensor_scalar(flat_index[:, :], flat_wrapped[:, :], 0.0, float(DIM1 * DIM2 - 1),
                                    ALU.max, ALU.min).then_inc(flat_index_ready, 1)
            nc.vector.tensor_scalar(row_index[:, :], row_wrapped[:, :], 0.0, idr[:, LAST_C:LAST_C + 1],
                                    ALU.max, ALU.min).then_inc(row_index_done, 1)

            cat_tab = tab[:, 0:CHUNKS * CAT].rearrange("p (k d) -> p k d", d=CAT)
            dve.wait_ge(s_tab, 16)
            dve.wait_ge(part_hi_done, 1)
            nc.vector.tensor_tensor(rest1[:, :, :], cat_tab, cat_parts[:, :, 0, :], ALU.subtract)\
                .then_inc(rest1_done, 1)

            dve.wait_ge(row_index_done, 1)
            nc.vector.tensor_scalar(row_hi[:, :], row_index[:, :], idr[:, SHIFT_C:SHIFT_C + 1], None,
                                    ALU.logical_shift_right).then_inc(row_hi_done, 1)
            dve.wait_ge(index_ready, 1)
            nc.vector.tensor_scalar(lo_index[:, :], index[:, TILES:], LO - 1, None, ALU.bitwise_and)\
                .then_inc(lo_index_done, 1)
            dve.wait_ge(row_hi_done, 1)
            nc.vector.tensor_scalar(row_hi16[:, :], row_hi[:, :], idr[:, START_C:START_C + 1], None, ALU.add)\
                .then_inc(row_hi16_ready, 1)
            dve.wait_ge(iota_ready, 2)
            dve.wait_ge(lo_index_done, 1)
            nc.vector.tensor_tensor(lo_hot[:, :, :],
                                    lo_index[:, :].unsqueeze(2).to_broadcast([P, WIDE * TILES, LO]),
                                    lo_iota[:, :].unsqueeze(1).to_broadcast([P, WIDE * TILES, LO]),
                                    ALU.is_equal).then_inc(lo_hot_ready, 1)
            dve.wait_ge(part_mid_done, 1)
            nc.vector.tensor_tensor(cat_parts[:, :, 2, :], rest1[:, :, :], cat_parts[:, :, 1, :], ALU.subtract)\
                .then_inc(part_lo_done, 1)

            dve.wait_ge(cat_ids_ready, 1)
            for k in range(CHUNKS):
                nc.vector.tensor_scalar(cat_hot[:, k, :], cat_ids[:, :], chunk_row[:, k:k + 1], None, ALU.is_equal)\
                    .then_inc(cat_hot_ready, 1)

            dve.wait_ge(hi_ids_ready, 1)
            nc.vector.tensor_scalar(hi_hot[:, :], hi_ids[:, :], chunk_row[:, 0:1], None, ALU.is_equal)\
                .then_inc(hi_hot_ready, 1)

            dve.wait_ge(s_w, 16)
            nc.vector.scalar_tensor_tensor(
                wf[:, 0:2 * H1].rearrange("p (a n) -> p a n", a=2), w[:, 0:2 * H1].rearrange("p (a n) -> p a n", a=2),
                BN_SCALE, w[:, GAIN:GAIN + H1].unsqueeze(1).to_broadcast([P, 2, H1]), ALU.mult, ALU.mult)\
                .then_inc(wf1_ready, 1)
            nc.vector.scalar_tensor_tensor(gain_bias[:, :], w[:, GAIN_COL:GAIN_COL + 3], BN_SCALE,
                                           w[:, BIAS_COL:BIAS_COL + 3], ALU.mult, ALU.mult)\
                .then_inc(gain_bias_done, 1)
            nc.vector.scalar_tensor_tensor(wf[:, W2C:W4C], w[:, W2C:W4C], BN_SCALE,
                                           w[:, GAIN + H1:GAIN + H1 + H2 + H3], ALU.mult, ALU.mult)\
                .then_inc(wf23_ready, 1)
            dve.wait_ge(gain_bias_done, 1)
            nc.vector.tensor_tensor(shift[:, :], gain_bias[:, :], w[:, BETA_COL:BETA_COL + 3], ALU.add)\
                .then_inc(shift_ready, 1)

            def item_features(t):
                dve.wait_ge(item_ps_ready[0], t // 2 + 1)
                nc.vector.tensor_copy(xa[0:ITEM, cols(t)], item_ps[0][0:ITEM, blk(t)]).then_inc(item_ready[0], 1)

            item_features(0)
            dve.wait_ge(lo_hot_ready, 1)
            dve.wait_ge(wide_ps_ready, 1)
            nc.vector.tensor_tensor(picked[:, :, :].rearrange("p t (a l) -> p t a l", a=WIDE),
                                    wide_ps[:, 0:TILES * WIDE * LO].rearrange("p (t a l) -> p t a l", t=TILES, a=WIDE),
                                    lo_hot[:, :, :].rearrange("p (a t) l -> p t a l", a=WIDE),
                                    ALU.mult).then_inc(picked_done, 1)
            item_features(2)
            dve.wait_ge(picked_done, 1)
            nc.vector.tensor_reduce(wide[:, :], picked[:, :, :], AX.X, ALU.add).then_inc(wide_ready, 1)

            dve.wait_ge(shift_ready, 1)
            for step in range(TILES // 2 + 2):
                for layer in (2, 1, 0):
                    t = 2 * (step - layer)
                    if 0 <= t < TILES:
                        h, ps, n = layers[layer]
                        dve.wait_ge(h_ps_ready[layer][0], t // 2 + 1)
                        nc.vector.tensor_scalar(h[0:n, cols(t)], ps[0][0:n, blk(t)], shift[0:n, layer:layer + 1], 0.0,
                                                ALU.add, ALU.max).then_inc(h_ready[layer][0], 1)

            dve.wait_ge(wide_ready, 1)
            dve.wait_ge(deep_ready, 1)
            nc.vector.tensor_tensor(deep_wide[:, :], deep_ps[:, 0:TILES], wide[:, :], ALU.add)\
                .then_inc(deep_wide_done, 1)
            dve.wait_ge(deep_wide_done, 1)
            dve.wait_ge(s_cross, 16 * TILES)
            nc.vector.tensor_tensor(total[:, :], deep_wide[:, :], cross[:, :], ALU.add).then_inc(total_ready, 1)

        @block.tensor
        def _(pe):
            pe.wait_ge(blank_ready, 1)
            for _ in range(WARM_UP):
                nc.tensor.matmul(warm_ps[:, :], blank[:, :], blank[:, :].unsqueeze(1).to_broadcast([P, TILES, P]),
                                 start=True, stop=True)

            pe.wait_ge(ident16_ready, 1)
            pe.wait_ge(row16_ready, 1)
            for t in range(TILES):
                last = nc.tensor.matmul(cat_bc[:, cols(t)], ident16[:, t:t + 1].to_broadcast([ROWS, P]),
                                        row16[:, :], start=True, stop=True)
            last.then_inc(cat_bc_ready, 1)
            pe.wait_ge(row_hi16_ready, 1)
            for a in range(WIDE):
                for t in range(TILES):
                    row = (a + 1) * TILES + t
                    last = nc.tensor.matmul(hi_bc[a * HALF:(a + 1) * HALF, cols(t)],
                                            ident16[:, row:row + 1].to_broadcast([ROWS, HALF]),
                                            row_hi16[:, :], start=True, stop=True)
            last.then_inc(hi_bc_ready, 1)

            pe.wait_ge(part_hi_done, 1)
            pe.wait_ge(part_mid_done, 1)
            pe.wait_ge(part_lo_done, 1)
            for k in range(CHUNKS):
                pe.wait_ge(cat_hot_ready, k + 1)
                last = nc.tensor.matmul(cat_ps[0:PARTS * CAT, :], cat_parts[:, k, :, :], cat_hot[:, k, :],
                                        start=(k == 0), stop=(k == CHUNKS - 1))
            last.then_inc(cat_ps_ready, 1)

            def transpose(t):
                pe.wait_ge(s_item[t], 16)
                if t >= 2:
                    pe.wait_ge(item_ready[t % 2], t // 2)
                nc.tensor.transpose(item_ps[t % 2][0:ITEM, blk(t)], item_rows[:, t, :], ident[:, :])\
                    .then_inc(item_ps_ready[t % 2], 1)

            pe.wait_ge(ident_ready, 1)
            transpose(0)
            transpose(1)

            wide_tab = tab[:, CHUNKS * CAT:TABLES]
            pe.wait_ge(s_tab, 16)
            pe.wait_ge(hi_hot_ready, 1)
            for t in range(TILES):
                last = nc.tensor.matmul(wide_ps[:, t * WIDE * LO:(t + 1) * WIDE * LO], hi_hot[:, cols(t)], wide_tab,
                                        start=True, stop=True)
            last.then_inc(wide_ps_ready, 1)

            pe.wait_ge(wf1_ready, 1)
            pe.wait_ge(s_price, 16)
            pe.wait_ge(xb_ready, 1)
            for e in range(2):
                nc.tensor.matmul(h1_ps[e][:, 0:2 * P], wf[0:XB, W1B:W1B + H1], parity(xb[:, :], e),
                                 start=True, stop=False, skip_group_check=True)
            transpose(2)
            transpose(3)

            def layer1(t):
                e, n = t % 2, t // 2
                pe.wait_ge(s_user, 16)
                pe.wait_ge(item_ready[e], n + 1)
                if n:
                    pe.wait_ge(h_ready[0][e], n)
                nc.tensor.matmul(h1_ps[e][:, blk(t)], wf[:, W1A:W1A + H1], xa[:, cols(t)],
                                 start=False, stop=True, skip_group_check=True).then_inc(h_ps_ready[0][e], 1)

            def layer2(t):
                e, n = t % 2, t // 2
                pe.wait_ge(wf23_ready, 1)
                pe.wait_ge(h_ready[0][e], n + 1)
                pe.wait_ge(hi_ids_ready, 1)
                if n:
                    pe.wait_ge(h_ready[1][e], n)
                nc.tensor.matmul(h2_ps[e][0:H2, blk(t)], wf[:, W2C:W2C + H2], h1[:, cols(t)],
                                 start=True, stop=True).then_inc(h_ps_ready[1][e], 1)

            def layer3(t):
                e, n = t % 2, t // 2
                pe.wait_ge(h_ready[1][e], n + 1)
                pe.wait_ge(picked_done, 1)
                if n:
                    pe.wait_ge(h_ready[2][e], n)
                nc.tensor.matmul(h3_ps[e][0:H3, blk(t)], wf[0:H2, W3C:W3C + H3], h2[:, cols(t)],
                                 start=True, stop=True).then_inc(h_ps_ready[2][e], 1)

            layer = [layer1, layer2, layer3]
            for step in range(TILES // 2 + 2):
                for n in (2, 1, 0):
                    for e in range(2):
                        t = 2 * (step - n) + e
                        if 0 <= t < TILES:
                            layer[n](t)

            pe.wait_ge(s_w, 16)
            pe.wait_ge(ones_ready, 1)
            for t in range(TILES):
                pe.wait_ge(h_ready[2][t % 2], t // 2 + 1)
                last = nc.tensor.matmul(deep_ps[:, t:t + 1], h3[:, cols(t)], w[0:H3 + 1, W4C:W4C + 1],
                                        start=True, stop=True)
            last.then_inc(deep_ready, 1)


def kernel(**inputs):
    import numpy as np
    import concourse.bacc as bacc
    from concourse.bass_utils import run_bass_kernel_spmd

    g = {k.replace("L0_rec_", ""): np.asarray(v) for k, v in inputs.items()}

    def tiles(ids):
        return ids.reshape(TILES, P)

    def rows(a, n=P):
        return np.pad(a, ((0, n - a.shape[0]), (0, 0)))

    id_cols = np.concatenate([tiles(g[k]).T for k in ("r_item_ids", "r_wf1", "r_wf2")], axis=1)
    size = np.repeat(np.array([CATS, DIM1, DIM2], np.int32), TILES)
    last = np.repeat(np.array([CATS - 1, DIM1 - 1, DIM2 - 1], np.int32), TILES)
    cut = np.repeat(np.array([0, LO_BITS, LO_BITS], np.int32), TILES)
    start = np.repeat(np.array([0, 0, HALF], np.int32), TILES)
    id_rows = np.concatenate([np.concatenate([tiles(g[k]) for k in ("r_category_ids", "r_wf1", "r_wf2")], axis=0),
                              size[:, None], last[:, None], cut[:, None], start[:, None]], axis=1)
    price_time = np.concatenate([g["r_price_features"].T, g["r_temporal_features"].T], axis=0)

    cat = rows(g["cat_emb"], CHUNKS * P).reshape(CHUNKS, P, CAT).transpose(1, 0, 2).reshape(P, CHUNKS * CAT)
    wide = [rows(g[k], HALF * LO).reshape(HALF, LO) for k in ("wide_emb1", "wide_emb2")]
    blank = np.zeros((HALF, LO), np.float32)
    tables = np.concatenate([cat, np.block([[wide[0], blank], [blank, wide[1]]])], axis=1)

    w1 = g["W1"]
    w1_user, w1_item, w1_cat, w1_rest = np.split(w1, [USER, USER + ITEM, USER + ITEM + CAT])
    gains = np.concatenate([g["g1"], g["g2"], g["g3"]])
    columns = [rows(g[f"{k}{i}"][:, None]) for k in ("b", "g", "be") for i in (1, 2, 3)]
    packed = np.concatenate(
        [np.concatenate([w1_item, w1_user]), rows(np.concatenate([w1_cat] * PARTS + [w1_rest])),
         rows(g["W2"]), rows(g["W3"]), rows(np.concatenate([g["W4"], g["b4"][None, :]])),
         np.broadcast_to(gains, (P, gains.shape[0]))] + columns, axis=1)

    arrays = {"id_cols": id_cols, "id_rows": id_rows, "user": g["r_user_embeddings"].T, "price_time": price_time, "tables": tables, "packed": packed,
              "item_emb": g["item_emb"], "cross_w": g["cross_W"].reshape(-1, 1)}
    arrays = {k: np.ascontiguousarray(v) for k, v in arrays.items()}

    nc = bacc.Bacc("TRN2", target_bir_lowering=False, num_devices=1)
    aps = [nc.dram_tensor(k, v.shape, mybir.dt.from_np(v.dtype), kind="ExternalInput").ap() for k, v in arrays.items()]
    out = nc.dram_tensor("out", (P, TILES), mybir.dt.float32, kind="ExternalOutput").ap()
    wide_deep_kernel(nc, *aps, out)
    r = run_bass_kernel_spmd(nc, [arrays], core_ids=[0])
    return r.results[0]["out"].T.reshape(B, 1)
```

```python
import concourse.bass as bass
from concourse import mybir
from contextlib import ExitStack

P = 128
B = 512
TILES = B // P
USER, ITEM, CAT, PRICE, TIME = 64, 64, 32, 2, 2
ITEMS, CATS, DIM1, DIM2 = 125000, 1001, 1250, 1250
H1, H2, H3 = 128, 64, 32
BN_EPS = 1e-05
BN_SCALE = (1.0 + BN_EPS) ** -0.5

PARTS = 3
CHUNKS = -(-CATS // P)
LO = 32
LO_BITS = LO.bit_length() - 1
HALF = P // 2
WIDE = 2

W1A, W1B = 0, H1
W2C = 2 * H1
W3C = W2C + H2
FOLDED = W3C + H3
GAIN = FOLDED
BETA3 = GAIN + H1 + H2 + H3
W4C = BETA3 + H3
B4C = W4C + H3
BIAS_COL = B4C + 1
GAIN_COL, BETA_COL = BIAS_COL + 2, BIAS_COL + 4
PACKED = BIAS_COL + 6
XA = ITEM + USER
XB = PARTS * CAT + PRICE + TIME
TABLES = CHUNKS * CAT + WIDE * LO
HALVES = 2
HB = B // HALVES
GROUPS = [(0, 2), (2, 3), (3, 4)]
WARM_UP = 8
FIRST_CHUNKS = 3
FILL = 3


def wide_deep_kernel(nc, id_cols, id_rows, user, price_time, tables, packed, item_emb, crosloaded_w, out):
    f32, bf16, f16, i32 = mybir.dt.float32, mybir.dt.bfloat16, mybir.dt.float16, mybir.dt.int32
    ALU, ACT, AX = mybir.AluOpType, mybir.ActivationFunctionType, mybir.AxisListType

    ctx = ExitStack()
    with ctx:
        def sb(name, shape, dt):
            return ctx.enter_context(nc.sbuf_tensor(name, shape, dt))

        def sem(name):
            return ctx.enter_context(nc.semaphore(name))

        idc = sb("idc", [P, 3 * TILES], i32)
        idr = sb("idr", [TILES, P], i32)
        tab = sb("tab", [P, TABLES], f32)
        w = sb("w", [P, PACKED], f32)
        item_rows = sb("item_rows", [P, TILES, ITEM], f32)
        cross = sb("cross", [P, TILES], f32)
        blank = sb("blank", [P, 16], bf16)
        ident = sb("ident", [P, P], f32)
        ident16 = sb("ident16", [TILES, TILES], f16)
        ident_bf = sb("ident_bf", [P, P], bf16)
        minus_row = sb("minus_row", [P, 1], f32)
        lo_iota = sb("lo_iota", [P, LO], i32)
        hi_iota = sb("hi_iota", [P, HALF], i32)
        dim2 = sb("dim2", [P, TILES], i32)
        wrap = sb("wrap", [P, 3 * TILES], f32)
        clamped = sb("clamped", [P, 3 * TILES], f32)
        index = sb("index", [P, 3 * TILES], i32)
        hi_index = sb("hi_index", [P, WIDE * TILES], i32)
        lo_index = sb("lo_index", [P, WIDE * TILES], i32)
        flat_product = sb("flat_product", [P, TILES], i32)
        flat = sb("flat", [P, TILES], i32)
        flat_wrap = sb("flat_wrap", [P, TILES], f32)
        flat_clamped = sb("flat_clamped", [P, TILES], f32)
        flat_index = sb("flat_index", [P, TILES], i32)
        row_wrap = sb("row_wrap", [TILES, P], f32)
        row_clamped = sb("row_clamped", [TILES, P], f32)
        row16 = sb("row16", [TILES, P], f16)
        cat_ids = sb("cat_ids", [P, B], f16)
        cat_hot = sb("cat_hot", [P, CHUNKS, B], bf16)
        hi_hot_t = sb("hi_hot_t", [P, TILES, WIDE, HALF], bf16)
        hi_hot = sb("hi_hot", [P, B], f32)
        lo_hot = sb("lo_hot", [P, WIDE * TILES, LO], f32)
        cat_parts = sb("cat_parts", [P, CHUNKS, PARTS, CAT], bf16)
        rest1 = sb("rest1", [P, CHUNKS, CAT], f32)
        picked = sb("picked", [P, TILES, WIDE * LO], f32)
        wf = sb("wf", [P, FOLDED], f32)
        gain_bias = sb("gain_bias", [P, 2], f32)
        shift = sb("shift", [P, 2], f32)
        xa = sb("xa", [XA, B], f32)
        xb = sb("xb", [XB, B], f32)
        h1 = sb("h1", [H1, B], f32)
        h2 = sb("h2", [H2 + 1, B], f32)
        terms = sb("terms", [P, TILES, H3 + 2], f32)
        table_loaded = sb("table_loaded", [1, 1], f32)
        deep_wide = sb("deep_wide", [P, TILES], f32)
        total = sb("total", [P, TILES], f32)

        bank = [ctx.enter_context(nc.psum_tensor(f"bank{i}", [P, 512], f32)) for i in range(8)]
        cat_bc, hi_ps = bank[0], bank[1][:, 0:B // 2].bitcast(bf16)
        cat_ps = [bank[2], bank[3]]
        item_ps = [bank[6], bank[7], bank[6][:, HB:]]
        warm_ps = bank[7]
        wide_ps = [bank[1][:, 0:TILES // 2 * WIDE * LO], bank[7][:, HB:HB + TILES // 2 * WIDE * LO]]
        h1_ps = [bank[4], bank[5], bank[0]]
        h2_ps = [bank[2], bank[3], bank[6]]
        h3_ps = [bank[4], bank[5], bank[0]]
        layers = [(h1, h1_ps, H1), (h2, h2_ps, H2)]

        def cols(t):
            return slice(t * P, (t + 1) * P)

        def half(h):
            return slice(h * HB, (h + 1) * HB)

        def users(g):
            return slice(GROUPS[g][0] * P, GROUPS[g][1] * P)

        def count(g):
            return (GROUPS[g][1] - GROUPS[g][0]) * P

        def sems(name, n):
            return [sem(f"{name}{i}") for i in range(n)]

        loaded_idc, loaded_idr, loaded_user, loaded_price, loaded_tab, loaded_w = (
            sem(f"loaded_{n}") for n in ("idc", "idr", "user", "price", "tab", "w"))
        item_landed = sems("item_landed", TILES)
        cross_landed, out_landed = sem("cross_landed"), sem("out_landed")
        blank_ready, ident0, ident_ready, ident16_ready = sem("blank_ready"), sem("ident0"), sem("ident_ready"), sem("ident16_ready")
        ident_bf_ready = sem("ident_bf_ready")
        dim2_ready, iota_ready, ones_ready = sem("dim2_ready"), sem("iota_ready"), sem("ones_ready")
        wrap_done, wide_wrap_done = sem("wrap_done"), sem("wide_wrap_done")
        index_ready, wide_index_ready = sem("index_ready"), sem("wide_index_ready")
        hi_index_done, lo_index_done, lo_hot_ready = sem("hi_index_done"), sem("lo_index_done"), sem("lo_hot_ready")
        product_done, flat_ready = sem("product_done"), sem("flat_ready")
        flat_wrap_done, flat_index_ready = sem("flat_wrap_done"), sem("flat_index_ready")
        row_wrap_done, row16_ready = sem("row_wrap_done"), sem("row16_ready")
        cat_bc_ready, cat_ids_ready, cat_hot_ready = sem("cat_bc_ready"), sem("cat_ids_ready"), sem("cat_hot_ready")
        hi_hot_t_ready, hi_ps_ready, hi_hot_ready = sem("hi_hot_t_ready"), sem("hi_ps_ready"), sem("hi_hot_ready")
        part_hi_done, rest1_done, part_mid_done, part_lo_done = sem("part_hi_done"), sem("rest1_done"), sem("part_mid_done"), sem("part_lo_done")
        picked_done = sem("picked_done")
        wf1_ready, wf23_done, wf23_ready, gain_bias_done, shift_ready = sem("wf1_ready"), sem("wf23_done"), sem("wf23_ready"), sem("gain_bias_done"), sem("shift_ready")
        terms_done, deep_wide_done, total_ready = sem("terms_done"), sem("deep_wide_done"), sem("total_ready")
        wide_ps_ready = sems("wide_ps_ready", HALVES)
        cat_ps_ready, xb_ready = sems("cat_ps_ready", HALVES), sems("xb_ready", HALVES)
        item_ps_ready, xa_ready = sems("item_ps_ready", len(GROUPS)), sems("xa_ready", len(GROUPS))
        h_ps_ready = [sems(f"h{n}_ps_ready", len(GROUPS)) for n in (1, 2, 3)]
        h_ready = [sems(f"h{n}_ready", len(GROUPS)) for n in (1, 2)]

        block = ctx.enter_context(nc.Block())

        @block.sync
        def _(sp):
            sp.dma_start(idc[:, :], id_cols).then_inc(loaded_idc, 16)
            sp.dma_start(idr[:, :], id_rows).then_inc(loaded_idr, 16)
            sp.dma_start(w[:, :], packed).then_inc(loaded_w, 16)
            sp.dma_start(xb[PARTS * CAT:XB, :], price_time).then_inc(loaded_price, 16)
            sp.dma_start(xa[ITEM:XA, :], user).then_inc(loaded_user, 16)
            sp.wait_ge(total_ready, 1)
            sp.dma_start(out, total[:, :]).then_inc(out_landed, 16)
            sp.wait_ge(out_landed, 16)

        @block.gpsimd
        def _(pool):
            pool.dma_start(tab[:, :], tables).then_inc(loaded_tab, 16)
            pool.memset(dim2[:, :], DIM2).then_inc(dim2_ready, 1)
            pool.memset(ident[:, :], 0.0).then_inc(ident0, 1)
            pool.iota(minus_row[:, :], pattern=[[0, 1]], base=0, channel_multiplier=-1,
                      allow_small_or_imprecise_dtypes=True).then_inc(iota_ready, 1)
            pool.iota(hi_iota[:, :], pattern=[[1, HALF]], base=0, channel_multiplier=0).then_inc(iota_ready, 1)
            pool.iota(lo_iota[:, :], pattern=[[1, LO]], base=0, channel_multiplier=0).then_inc(iota_ready, 1)
            pool.wait_ge(ident0, 1)
            pool.affine_select(out=ident[:, :], in_=ident[:, :], compare_op=ALU.not_equal, fill=1.0,
                               base=0, pattern=[[-1, P]], channel_multiplier=1).then_inc(ident_ready, 1)
            pool.wait_ge(loaded_idc, 16)
            pool.wait_ge(dim2_ready, 1)
            pool.tensor_tensor(flat_product[:, :], idc[:, TILES:2 * TILES], dim2[:, :], ALU.mult)\
                .then_inc(product_done, 1)
            pool.wait_ge(product_done, 1)
            pool.tensor_tensor(flat[:, :], flat_product[:, :], idc[:, 2 * TILES:], ALU.add).then_inc(flat_ready, 1)
            pool.wait_ge(index_ready, 1)
            for t in range(TILES):
                pool.indirect_dma_start(item_rows[:, t, :], None, item_emb,
                                        bass.IndirectOffsetOnAxis(index[:, t:t + 1], 0)).then_inc(item_landed[t], 16)
            pool.wait_ge(flat_index_ready, 1)
            for t in range(TILES):
                pool.indirect_dma_start(cross[:, t:t + 1], None, crosloaded_w,
                                        bass.IndirectOffsetOnAxis(flat_index[:, t:t + 1], 0)).then_inc(cross_landed, 16)

        @block.scalar
        def _(act):
            act.wait_ge(blank_ready, 1)
            nc.scalar.activation(table_loaded[:, :], blank[0:1, 0:1], ACT.Relu)
            act.wait_ge(ident_ready, 1)
            nc.scalar.activation(ident_bf[:, :], ident[:, :], ACT.Copy).then_inc(ident_bf_ready, 1)
            act.wait_ge(iota_ready, 3)
            act.wait_ge(cat_bc_ready, 1)
            nc.scalar.activation(cat_ids[:, :], cat_bc[:, :], ACT.Identity, bias=minus_row[:, 0:1])\
                .then_inc(cat_ids_ready, 1)
            act.wait_ge(hi_ps_ready, 1)
            nc.scalar.activation(hi_hot[:, :], hi_ps[:, :], ACT.Copy).then_inc(hi_hot_ready, 1)

            act.wait_ge(cat_ps_ready[0], 1)
            nc.scalar.activation(xb[0:PARTS * CAT, half(0)], cat_ps[0][0:PARTS * CAT, 0:HB], ACT.Copy)\
                .then_inc(xb_ready[0], 1)
            for g in range(len(GROUPS)):
                act.wait_ge(item_ps_ready[g], 1)
                nc.scalar.activation(xa[0:ITEM, users(g)], item_ps[g][0:ITEM, 0:count(g)], ACT.Copy)\
                    .then_inc(xa_ready[g], 1)
            act.wait_ge(shift_ready, 1)
            for layer, g in [(0, 1), (0, 2), (1, 1)]:
                h, ps, n = layers[layer]
                act.wait_ge(h_ps_ready[layer][g], 1)
                nc.scalar.activation(h[0:n, users(g)], ps[g][0:n, 0:count(g)], ACT.Relu,
                                     bias=shift[0:n, layer:layer + 1]).then_inc(h_ready[layer][g], 1)

        @block.vector
        def _(dve):
            nc.vector.memset(blank[:, :], 0.0).then_inc(blank_ready, 1)
            nc.vector.memset(h2[H2:H2 + 1, :], 1.0).then_inc(ones_ready, 1)

            dve.wait_ge(ident_ready, 1)
            nc.vector.tensor_copy(ident16[:, :], ident[0:TILES, 0:TILES]).then_inc(ident16_ready, 1)

            def wrap_and_clamp(ids, size, wrap, clamped, wrap_done):
                nc.vector.tensor_scalar(wrap, ids, 0.0, float(size), ALU.is_lt, ALU.mult)
                nc.vector.tensor_scalar(clamped, ids, float(-size), float(size - 1), ALU.max, ALU.min)\
                    .then_inc(wrap_done, 1)

            items, wides = slice(0, TILES), slice(TILES, 3 * TILES)
            dve.wait_ge(loaded_idc, 16)
            wrap_and_clamp(idc[:, items], ITEMS, wrap[:, items], clamped[:, items], wrap_done)
            wrap_and_clamp(idc[:, wides], DIM1, wrap[:, wides], clamped[:, wides], wide_wrap_done)
            dve.wait_ge(wrap_done, 1)
            nc.vector.tensor_tensor(index[:, items], wrap[:, items], clamped[:, items], ALU.add).then_inc(index_ready, 1)
            dve.wait_ge(loaded_idr, 16)
            wrap_and_clamp(idr[:, :], CATS, row_wrap[:, :], row_clamped[:, :], row_wrap_done)
            dve.wait_ge(wide_wrap_done, 1)
            nc.vector.tensor_tensor(index[:, wides], wrap[:, wides], clamped[:, wides], ALU.add)\
                .then_inc(wide_index_ready, 1)
            dve.wait_ge(row_wrap_done, 1)
            nc.vector.tensor_tensor(row16[:, :], row_wrap[:, :], row_clamped[:, :], ALU.add).then_inc(row16_ready, 1)
            cat_tab = tab[:, 0:CHUNKS * CAT].rearrange("p (k d) -> p k d", d=CAT)
            dve.wait_ge(loaded_tab, 16)
            nc.vector.tensor_copy(cat_parts[:, :, 0, :], cat_tab).then_inc(part_hi_done, 1)
            dve.wait_ge(flat_ready, 1)
            wrap_and_clamp(flat[:, :], DIM1 * DIM2, flat_wrap[:, :], flat_clamped[:, :], flat_wrap_done)
            dve.wait_ge(part_hi_done, 1)
            nc.vector.tensor_tensor(rest1[:, :, :], cat_tab, cat_parts[:, :, 0, :], ALU.subtract)\
                .then_inc(rest1_done, 1)
            dve.wait_ge(flat_wrap_done, 1)
            nc.vector.tensor_tensor(flat_index[:, :], flat_wrap[:, :], flat_clamped[:, :], ALU.add)\
                .then_inc(flat_index_ready, 1)
            dve.wait_ge(rest1_done, 1)
            nc.vector.tensor_copy(cat_parts[:, :, 1, :], rest1[:, :, :]).then_inc(part_mid_done, 1)
            dve.wait_ge(wide_index_ready, 1)
            nc.vector.tensor_scalar(hi_index[:, :], index[:, TILES:], LO_BITS, None, ALU.logical_shift_right)\
                .then_inc(hi_index_done, 1)
            dve.wait_ge(part_mid_done, 1)
            nc.vector.tensor_tensor(cat_parts[:, :, 2, :], rest1[:, :, :], cat_parts[:, :, 1, :], ALU.subtract)\
                .then_inc(part_lo_done, 1)

            def chunk_hot(k):
                nc.vector.tensor_scalar(cat_hot[:, k, :], cat_ids[:, :], float(k * P), None, ALU.is_equal)\
                    .then_inc(cat_hot_ready, 1)

            dve.wait_ge(cat_ids_ready, 1)
            for k in range(FIRST_CHUNKS):
                chunk_hot(k)
            dve.wait_ge(iota_ready, 3)
            dve.wait_ge(hi_index_done, 1)
            nc.vector.tensor_tensor(hi_hot_t[:, :, :, :].rearrange("p t a n -> p a t n"),
                                    hi_index[:, :].rearrange("p (a t) -> p a t", a=WIDE).unsqueeze(3)
                                    .to_broadcast([P, WIDE, TILES, HALF]),
                                    hi_iota[:, :].unsqueeze(1).unsqueeze(1).to_broadcast([P, WIDE, TILES, HALF]),
                                    ALU.is_equal).then_inc(hi_hot_t_ready, 1)
            for k in range(FIRST_CHUNKS, CHUNKS):
                chunk_hot(k)

            dve.wait_ge(loaded_w, 16)
            nc.vector.scalar_tensor_tensor(
                wf[:, 0:2 * H1].rearrange("p (a n) -> p a n", a=2), w[:, 0:2 * H1].rearrange("p (a n) -> p a n", a=2),
                BN_SCALE, w[:, GAIN:GAIN + H1].unsqueeze(1).to_broadcast([P, 2, H1]), ALU.mult, ALU.mult)\
                .then_inc(wf1_ready, 1)
            nc.vector.scalar_tensor_tensor(gain_bias[:, :], w[:, GAIN_COL:GAIN_COL + 2], BN_SCALE,
                                           w[:, BIAS_COL:BIAS_COL + 2], ALU.mult, ALU.mult)\
                .then_inc(gain_bias_done, 1)
            dve.wait_ge(gain_bias_done, 1)
            nc.vector.tensor_tensor(shift[:, :], gain_bias[:, :], w[:, BETA_COL:BETA_COL + 2], ALU.add)\
                .then_inc(shift_ready, 1)
            nc.vector.scalar_tensor_tensor(wf[:, W2C:FOLDED], w[:, W2C:FOLDED], BN_SCALE,
                                           w[:, GAIN + H1:GAIN + H1 + H2 + H3], ALU.mult, ALU.mult)\
                .then_inc(wf23_done, 1)

            nc.vector.tensor_copy(terms[:, :, H3 + 1], w[:, B4C:B4C + 1].to_broadcast([P, TILES])).then_inc(terms_done, 1)

            dve.wait_ge(cat_ps_ready[1], 1)
            nc.vector.tensor_copy(xb[0:PARTS * CAT, half(1)], cat_ps[1][0:PARTS * CAT, 0:HB]).then_inc(xb_ready[1], 1)

            nc.vector.tensor_scalar(lo_index[:, :], index[:, TILES:], LO - 1, None, ALU.bitwise_and)\
                .then_inc(lo_index_done, 1)
            dve.wait_ge(wf23_done, 1)
            nc.vector.tensor_tensor(wf[H2:H2 + 1, W3C:FOLDED], wf[H2:H2 + 1, W3C:FOLDED],
                                    w[H2:H2 + 1, BETA3:BETA3 + H3], ALU.add).then_inc(wf23_ready, 1)
            dve.wait_ge(lo_index_done, 1)
            nc.vector.tensor_tensor(lo_hot[:, :, :],
                                    lo_index[:, :].unsqueeze(2).to_broadcast([P, WIDE * TILES, LO]),
                                    lo_iota[:, :].unsqueeze(1).to_broadcast([P, WIDE * TILES, LO]),
                                    ALU.is_equal).then_inc(lo_hot_ready, 1)

            def relu(layer, g):
                h, ps, n = layers[layer]
                dve.wait_ge(h_ps_ready[layer][g], 1)
                nc.vector.tensor_scalar(h[0:n, users(g)], ps[g][0:n, 0:count(g)], shift[0:n, layer:layer + 1], 0.0,
                                        ALU.add, ALU.max).then_inc(h_ready[layer][g], 1)

            def last_terms(g):
                first, end = GROUPS[g]
                dve.wait_ge(h_ps_ready[2][g], 1)
                nc.vector.scalar_tensor_tensor(
                    terms[:, first:end, 0:H3],
                    h3_ps[g][:, 0:(end - first) * H3].rearrange("p (t n) -> p t n", n=H3), 0.0,
                    w[:, W4C:W4C + H3].unsqueeze(1).to_broadcast([P, end - first, H3]), ALU.max, ALU.mult)\
                    .then_inc(terms_done, 1)

            def pick(h):
                tiles = slice(h * TILES // HALVES, (h + 1) * TILES // HALVES)
                dve.wait_ge(wide_ps_ready[h], 1)
                nc.vector.tensor_tensor(picked[:, tiles, :].rearrange("p t (a l) -> p t a l", a=WIDE),
                                        wide_ps[h].rearrange("p (t a l) -> p t a l", a=WIDE, l=LO),
                                        lo_hot[:, :, :].rearrange("p (a t) l -> p t a l", a=WIDE)[:, tiles],
                                        ALU.mult).then_inc(picked_done, 1)

            def pick_sum(h):
                tiles = slice(h * TILES // HALVES, (h + 1) * TILES // HALVES)
                dve.wait_ge(picked_done, h + 1)
                nc.vector.tensor_reduce(terms[:, tiles, H3], picked[:, tiles, :], AX.X, ALU.add).then_inc(terms_done, 1)

            dve.wait_ge(lo_hot_ready, 1)
            pick(0)
            pick_sum(0)
            dve.wait_ge(shift_ready, 1)
            relu(0, 0)
            relu(1, 0)
            relu(1, 2)
            pick(1)
            pick_sum(1)
            for g in range(len(GROUPS)):
                last_terms(g)
            dve.wait_ge(terms_done, 1 + HALVES + len(GROUPS) - 1)
            nc.vector.tensor_reduce(deep_wide[:, 0:TILES - 1], terms[:, 0:TILES - 1, :], AX.X, ALU.add)
            dve.wait_ge(terms_done, 1 + HALVES + len(GROUPS))
            nc.vector.tensor_reduce(deep_wide[:, TILES - 1:], terms[:, TILES - 1:, :], AX.X, ALU.add)\
                .then_inc(deep_wide_done, 1)
            dve.wait_ge(deep_wide_done, 1)
            dve.wait_ge(cross_landed, 16 * TILES)
            nc.vector.tensor_tensor(total[:, :], deep_wide[:, :], cross[:, :], ALU.add).then_inc(total_ready, 1)

        @block.tensor
        def _(pe):
            ones_row = nc.const_aps.tensor(1.0, [P, P], bf16)
            ones_cols = nc.const_aps.tensor(1.0, [P, B], bf16)

            def keep_warm(n):
                for _ in range(n):
                    nc.tensor.matmul(warm_ps[:, :], ones_row, ones_cols, start=True, stop=True)

            keep_warm(WARM_UP)

            pe.wait_ge(ident16_ready, 1)
            pe.wait_ge(row16_ready, 1)
            for t in range(TILES):
                last = nc.tensor.matmul(cat_bc[:, cols(t)], ident16[:, t:t + 1].to_broadcast([TILES, P]),
                                        row16[:, :], start=True, stop=True)
            last.then_inc(cat_bc_ready, 1)
            keep_warm(FILL)
            def cat_chunk(k):
                pe.wait_ge(cat_hot_ready, k + 1)
                for h in range(HALVES):
                    last = nc.tensor.matmul(cat_ps[h][0:PARTS * CAT, 0:HB], cat_parts[:, k, :, :],
                                            cat_hot[:, k, half(h)], start=(k == 0), stop=(k == CHUNKS - 1))
                    if k == CHUNKS - 1:
                        last.then_inc(cat_ps_ready[h], 1)

            def hi_transposes():
                pe.wait_ge(ident_bf_ready, 1)
                pe.wait_ge(hi_hot_t_ready, 1)
                for t in range(TILES):
                    last = nc.tensor.transpose(hi_ps[:, cols(t)], hi_hot_t[:, t, :, :].rearrange("p a n -> p (a n)"),
                                               ident_bf[:, :])
                last.then_inc(hi_ps_ready, 1)

            def gathered(g):
                first, end = GROUPS[g]
                if g == 2:
                    pe.wait_ge(xa_ready[0], 1)
                for t in range(first, end):
                    pe.wait_ge(item_landed[t], 16)
                    last = nc.tensor.transpose(item_ps[g][0:ITEM, cols(t - first)], item_rows[:, t, :], ident[:, :])
                last.then_inc(item_ps_ready[g], 1)

            def wide_candidates(h):
                pe.wait_ge(loaded_tab, 16)
                pe.wait_ge(hi_hot_ready, 1)
                for t in range(TILES // HALVES):
                    last = nc.tensor.matmul(wide_ps[h][:, t * WIDE * LO:(t + 1) * WIDE * LO],
                                            hi_hot[:, cols(h * TILES // HALVES + t)],
                                            tab[:, CHUNKS * CAT:TABLES], start=True, stop=True)
                last.then_inc(wide_ps_ready[h], 1)

            def layer1_cat(g):
                pe.wait_ge(wf1_ready, 1)
                pe.wait_ge(loaded_price, 16)
                pe.wait_ge(xb_ready[GROUPS[g][0] * HALVES // TILES], 1)
                nc.tensor.matmul(h1_ps[g][:, 0:count(g)], wf[0:XB, W1B:W1B + H1], xb[:, users(g)],
                                 start=True, stop=False, skip_group_check=True)

            def layer1_item(g):
                pe.wait_ge(loaded_user, 16)
                pe.wait_ge(xa_ready[g], 1)
                nc.tensor.matmul(h1_ps[g][:, 0:count(g)], wf[:, W1A:W1A + H1], xa[:, users(g)],
                                 start=False, stop=True, skip_group_check=True).then_inc(h_ps_ready[0][g], 1)

            def layer2(g):
                pe.wait_ge(wf23_ready, 1)
                pe.wait_ge(h_ready[0][g], 1)
                nc.tensor.matmul(h2_ps[g][0:H2, 0:count(g)], wf[:, W2C:W2C + H2], h1[:, users(g)],
                                 start=True, stop=True).then_inc(h_ps_ready[1][g], 1)

            def layer3(g):
                first, end = GROUPS[g]
                pe.wait_ge(ones_ready, 1)
                pe.wait_ge(h_ready[1][g], 1)
                for t in range(first, end):
                    last = nc.tensor.matmul(h3_ps[g][:, (t - first) * H3:(t - first + 1) * H3], h2[:, cols(t)],
                                            wf[0:H2 + 1, W3C:FOLDED], start=True, stop=True)
                last.then_inc(h_ps_ready[2][g], 1)

            pe.wait_ge(part_hi_done, 1)
            pe.wait_ge(part_mid_done, 1)
            pe.wait_ge(part_lo_done, 1)
            for k in range(FIRST_CHUNKS):
                cat_chunk(k)
            hi_transposes()
            for k in range(FIRST_CHUNKS, CHUNKS):
                cat_chunk(k)
            gathered(0)
            wide_candidates(0)
            layer1_cat(0)
            gathered(1)
            layer1_item(0)
            gathered(2)
            layer1_cat(1)
            layer1_item(1)
            layer1_cat(2)
            layer1_item(2)
            layer2(0)
            layer2(1)
            layer2(2)
            wide_candidates(1)
            layer3(0)
            layer3(1)
            layer3(2)


def kernel(**inputs):
    import numpy as np
    import concourse.bacc as bacc
    from concourse.bass_utils import run_bass_kernel_spmd

    g = {k.replace("L0_rec_", ""): np.asarray(v) for k, v in inputs.items()}

    def tiles(ids):
        return ids.reshape(TILES, P)

    def rows(a, n=P):
        return np.pad(a, ((0, n - a.shape[0]), (0, 0)))

    id_cols = np.concatenate([tiles(g[k]).T for k in ("r_item_ids", "r_wf1", "r_wf2")], axis=1)
    id_rows = tiles(g["r_category_ids"])
    price_time = np.concatenate([g["r_price_features"].T, g["r_temporal_features"].T], axis=0)

    cat = rows(g["cat_emb"], CHUNKS * P).reshape(CHUNKS, P, CAT).transpose(1, 0, 2).reshape(P, CHUNKS * CAT)
    wide = [rows(g[k], HALF * LO).reshape(HALF, LO) for k in ("wide_emb1", "wide_emb2")]
    blank = np.zeros((HALF, LO), np.float32)
    tables = np.concatenate([cat, np.block([[wide[0], blank], [blank, wide[1]]])], axis=1)

    w1 = g["W1"]
    w1_user, w1_item, w1_cat, w1_rest = np.split(w1, [USER, USER + ITEM, USER + ITEM + CAT])
    gains = np.concatenate([g["g1"], g["g2"], g["g3"]])
    columns = [rows(g[f"{k}{i}"][:, None]) for k in ("b", "g", "be") for i in (1, 2)]

    def everywhere(a):
        return np.broadcast_to(a.reshape(1, -1), (P, a.size))

    w3 = rows(np.concatenate([g["W3"], g["b3"][None, :]]))
    packed = np.concatenate(
        [np.concatenate([w1_item, w1_user]), rows(np.concatenate([w1_cat] * PARTS + [w1_rest])),
         rows(g["W2"]), w3, everywhere(gains), everywhere(g["be3"]), everywhere(g["W4"]), everywhere(g["b4"])]
        + columns, axis=1)

    arrays = {"id_cols": id_cols, "id_rows": id_rows, "user": g["r_user_embeddings"].T, "price_time": price_time, "tables": tables, "packed": packed,
              "item_emb": g["item_emb"], "cross_w": g["cross_W"].reshape(-1, 1)}
    arrays = {k: np.ascontiguousarray(v) for k, v in arrays.items()}

    nc = bacc.Bacc("TRN2", target_bir_lowering=False, num_devices=1)
    aps = [nc.dram_tensor(k, v.shape, mybir.dt.from_np(v.dtype), kind="ExternalInput").ap() for k, v in arrays.items()]
    out = nc.dram_tensor("out", (P, TILES), mybir.dt.float32, kind="ExternalOutput").ap()
    wide_deep_kernel(nc, *aps, out)
    r = run_bass_kernel_spmd(nc, [arrays], core_ids=[0])
    return r.results[0]["out"].T.reshape(B, 1)
```
